# Optimizing a Trainium2 kernel written in Bass

```python
import numpy as np
import jax
import jax.numpy as jnp

def _softmax(x, axis=-1):
    return jax.nn.softmax(x, axis=axis)

def _gelu(x):
    return jax.nn.gelu(x, approximate=True)

def _silu(x):
    return jax.nn.silu(x)

def _sigmoid(x):
    return jax.nn.sigmoid(x)

def _layernorm(x, axis=-1, eps=1e-05):
    m = jnp.mean(x, axis=axis, keepdims=True)
    v = jnp.var(x, axis=axis, keepdims=True)
    return (x - m) / jnp.sqrt(v + eps)

def _scatter_add(tgt, idx, src, axis=0):
    return tgt.at[idx].add(src)

def _segment_sum(src, seg, n):
    return jax.ops.segment_sum(src, seg, n)
kernel_name = 'mk_adj_resnorm_d1_adj_r2_0b89c5'

def setup_inputs(seed: int=0):
    np.random.seed(seed)
    _w = jnp.asarray

    def _rec_inputs():
        import jax
        import jax.numpy as jnp
        _gk = jax.random.key(seed)
        x = -0.0003929 + 0.9999 * jax.random.normal(jax.random.fold_in(_gk, 1), (16, 512, 256), jnp.float32)
        _a = jax.random.bernoulli(jax.random.fold_in(_gk, 2), 0.015625, (16, 512, 512))
        _a = jnp.logical_or(_a, jnp.swapaxes(_a, -1, -2))
        _a = jnp.logical_or(_a, jnp.eye(512, dtype=bool))
        _af = _a.astype(jnp.float32)
        _af = _af * jax.random.uniform(jax.random.fold_in(_gk, 3), (16, 512, 512), jnp.float32, 0.05, 1)
        adj = _af
        return (x, adj)
    x, adj = _rec_inputs()

    def _L0_gnn_setup():
        import jax, jax.numpy as jnp
        import numpy as np
        B, N, F_IN, F_HID, F_OUT = (32, 512, 256, 256, 256)

        def _gcn_layer(x, adj, W, b):
            support = jnp.einsum('bnf,fh->bnh', x, W)
            return jnp.einsum('bnm,bmh->bnh', adj, support) + b
        key = jax.random.key(seed)
        ks = jax.random.split(key, 8)

        def xavier(k, fan_in, fan_out):
            bound = float(np.sqrt(6.0 / (fan_in + fan_out)))
            return jax.random.uniform(k, (fan_in, fan_out), jnp.float32, -bound, bound)
        return {'batch_graph': jax.random.normal(ks[0], (B, N, F_IN), jnp.float32), 'adj': jax.random.uniform(ks[1], (B, N, N), jnp.float32), 'W1': xavier(ks[2], F_IN, F_HID), 'b1': jnp.zeros((F_HID,), jnp.float32), 'W2': xavier(ks[3], F_HID, F_HID), 'b2': jnp.zeros((F_HID,), jnp.float32), 'W3': xavier(ks[4], F_HID, F_OUT), 'b3': jnp.zeros((F_OUT,), jnp.float32)}
    _L0_gnn_all = _L0_gnn_setup()
    _L0_gnn_in = {k: v for k, v in _L0_gnn_all.items() if k in ('W1', 'b1', 'W2', 'b2', 'W3', 'b3')}
    del _L0_gnn_all
    return {'x': x, 'adj': adj, 'L0_gnn_W1': _L0_gnn_in['W1'], 'L0_gnn_b1': _L0_gnn_in['b1'], 'L0_gnn_W2': _L0_gnn_in['W2'], 'L0_gnn_b2': _L0_gnn_in['b2'], 'L0_gnn_W3': _L0_gnn_in['W3'], 'L0_gnn_b3': _L0_gnn_in['b3']}

def reference(x, adj, L0_gnn_W1, L0_gnn_b1, L0_gnn_W2, L0_gnn_b2, L0_gnn_W3, L0_gnn_b3):
    import jax
    import jax.numpy as jnp

    def _L0_gnn_ref(batch_graph, adj, W1, b1, W2, b2, W3, b3):
        import jax, jax.numpy as jnp
        import numpy as np
        B, N, F_IN, F_HID, F_OUT = (32, 512, 256, 256, 256)

        def _gcn_layer(x, adj, W, b):
            support = jnp.einsum('bnf,fh->bnh', x, W)
            return jnp.einsum('bnm,bmh->bnh', adj, support) + b
        x = jax.nn.relu(_gcn_layer(batch_graph, adj, W1, b1))
        x = jax.nn.relu(_gcn_layer(x, adj, W2, b2))
        out = _gcn_layer(x, adj, W3, b3)
        return out
    x = _layernorm(x + _L0_gnn_ref(x, adj, L0_gnn_W1, L0_gnn_b1, L0_gnn_W2, L0_gnn_b2, L0_gnn_W3, L0_gnn_b3), axis=-1)
    return x

_drawn_inputs = setup_inputs


def setup_inputs(seed=0):
    import zlib

    import numpy as np

    out = dict(_drawn_inputs(seed))
    spreads = {'L0_gnn_b1': (0.0, 0.1), 'L0_gnn_b2': (0.0, 0.8), 'L0_gnn_b3': (0.0, 2.0)}
    factors = {}
    for name, (base, spread) in spreads.items():
        noise = np.random.default_rng([zlib.crc32(name.encode()), seed]).standard_normal(out[name].shape)
        drawn = base * np.exp(spread * noise) if base else spread * noise
        out[name] = jnp.asarray(drawn.astype(out[name].dtype))
    for name, factor in factors.items():
        out[name] = (out[name] * factor).astype(out[name].dtype)
    return out
```

```python
from contextlib import ExitStack

import concourse.bass as bass
from concourse import mybir

P = 128
SLOTS = 3
SQ = 32
BANK = 512
EPS = 1e-5
DMA = 16

ALU = mybir.AluOpType
ACT = mybir.ActivationFunctionType
F32 = mybir.dt.float32
F32R = mybir.dt.float32r


def gcn_resnorm(nc, x, adj, W1, b1, W2, b2, W3, b3, out):
    B, N, F = x.shape
    MT = N // P
    FT = F // P
    HALVES = MT * F // BANK
    PER_BANK = MT // HALVES
    assert N == BANK and FT == HALVES == 2 and MT == 4
    ROUNDS = (B - 2) // SLOTS
    LOOPED = ROUNDS * SLOTS

    x_dram = x.rearrange("b (t p) f -> b p t f", p=P)
    adj_dram = adj.rearrange("b (t p) m -> b t p m", p=P)
    QUADS = P // SQ
    squares_dram = adj.rearrange("b (n j) (k a i) -> b a j k n i", j=SQ, a=QUADS, i=SQ)
    out_dram = out.rearrange("b (h t p) f -> b h p t f", p=P, h=HALVES)

    with ExitStack() as ctx:
        def sb(name, shape, dt=F32):
            return ctx.enter_context(nc.sbuf_tensor(name, shape, dt))

        def bank(name):
            return ctx.enter_context(nc.psum_tensor(name, [P, BANK], F32))

        def sem(name):
            return ctx.enter_context(nc.semaphore(name))

        ident = sb("ident", [P, P])
        w_raw = sb("w_raw", [P, 3, FT, F])
        w_hi = sb("w_hi", [P, 3, FT, F], F32R)
        w_lo = sb("w_lo", [P, 3, FT, F], F32R)
        b1_col = sb("b1_col", [P, FT])
        b2_col = sb("b2_col", [P, FT])
        b3_rows = sb("b3_rows", [P, MT, F])
        minus_half = sb("minus_half", [P, PER_BANK])
        adj_raw = [sb(f"adj_raw{s}", [P, MT, N]) for s in range(SLOTS)]
        adjT_hi = [sb(f"adjT_hi{s}", [P, MT, N], F32R) for s in range(SLOTS)]
        adjT_lo = [sb(f"adjT_lo{s}", [P, MT, N], F32R) for s in range(SLOTS)]
        x_rows = [sb(f"x_rows{s}", [P, MT, F]) for s in range(SLOTS)]
        x_hi = sb("x_hi", [P, MT, F], F32R)
        x_lo = sb("x_lo", [P, MT, F], F32R)
        axT_hi = sb("axT_hi", [P, FT, N], F32R)
        axT_lo = sb("axT_lo", [P, FT, N], F32R)
        h1T_hi = sb("h1T_hi", [P, FT, N], F32R)
        h1T_lo = sb("h1T_lo", [P, FT, N], F32R)
        h2T_hi = sb("h2T_hi", [P, FT, N], F32R)
        h2T_lo = sb("h2T_lo", [P, FT, N], F32R)
        s2_hi = sb("s2_hi", [P, MT, F], F32R)
        s2_lo = sb("s2_lo", [P, MT, F], F32R)
        s3_hi = sb("s3_hi", [P, MT, F], F32R)
        s3_lo = sb("s3_lo", [P, MT, F], F32R)
        y = [sb(f"y{s}", [P, MT, F]) for s in range(SLOTS)]
        stats = sb("stats", [P, MT, 6])
        mean_sum = sb("mean_sum", [P, MT])
        mean_gap = sb("mean_gap", [P, MT])
        squares = sb("squares", [P, MT])
        gap_square = sb("gap_square", [P, MT])
        mean = sb("mean", [P, MT])
        var_eps = sb("var_eps", [P, MT])
        rstd = sb("rstd", [P, MT])

        turned = [bank(f"turned{k}") for k in range(2)]
        acc_a = [bank(f"acc_a{k}") for k in range(2)]
        acc_b = [bank(f"acc_b{k}") for k in range(2)]
        acc_c = [bank(f"acc_c{k}") for k in range(2)]
        first_turned = turned + acc_b

        tile_loaded = [sem(f"tile_loaded{t}") for t in range(MT)]
        second_loaded = sem("second_loaded")
        adj_loaded = [sem(f"adj_loaded{s}") for s in range(SLOTS)]
        x_loaded = [sem(f"x_loaded{s}") for s in range(SLOTS)]
        w_loaded = [sem(f"w_loaded{n}") for n in range(3)]
        bias_loaded = sem("bias_loaded")
        stored = [sem(f"stored{s}") for s in range(SLOTS)]
        const_set = sem("const_set")
        ident_ready = sem("ident_ready")
        w_hi_ready, w_lo_ready = sem("w_hi_ready"), sem("w_lo_ready")
        x_hi_ready, x_lo_ready = sem("x_hi_ready"), sem("x_lo_ready")
        x_biased = sem("x_biased")
        squares_turned = sem("squares_turned")
        turn_done = sem("turn_done")
        ax_done, h1_done, s2_done = sem("ax_done"), sem("h1_done"), sem("s2_done")
        h2_done, s3_done, y_done = sem("h2_done"), sem("s3_done"), sem("y_done")
        adjT_hi_ready, adjT_lo_ready = sem("adjT_hi_ready"), sem("adjT_lo_ready")
        ax_hi_ready, ax_lo_ready = sem("ax_hi_ready"), sem("ax_lo_ready")
        h1_hi_ready, h1_lo_ready = sem("h1_hi_ready"), sem("h1_lo_ready")
        s2_hi_ready, s2_lo_ready = sem("s2_hi_ready"), sem("s2_lo_ready")
        h2_hi_ready, h2_lo_ready = sem("h2_hi_ready"), sem("h2_lo_ready")
        s3_hi_ready, s3_lo_ready = sem("s3_hi_ready"), sem("s3_lo_ready")
        h1_relu_done, h2_relu_done = sem("h1_relu_done"), sem("h2_relu_done")
        y_added = sem("y_added")
        stats_done, pair_done = sem("stats_done"), sem("pair_done")
        gap_done, mean_ready, var_ready = sem("gap_done"), sem("mean_ready"), sem("var_ready")
        rstd_ready, y_normed = sem("rstd_ready"), sem("y_normed")

        def graph(r, u):
            return r * SLOTS + u

        def dma_count(r, u):
            return DMA * (r + u // SLOTS + 1)

        block = ctx.enter_context(nc.Block())

        @block.sync
        def _(sp):
            def load_adj(r, u):
                s, c = u % SLOTS, graph(r, u)
                for a in range(QUADS):
                    part = adj_raw[s][a * SQ:(a + 1) * SQ].rearrange("j k (n i) -> j k n i", i=SQ)
                    sp.dma_start(part, squares_dram[c, a]).then_inc(adj_loaded[s], DMA)

            def load_x(r, u):
                sp.dma_start(x_rows[u % SLOTS][:], x_dram[graph(r, u)]).then_inc(x_loaded[u % SLOTS], DMA)

            def load_w(n, w):
                sp.dma_start(w_raw[:, n], w.rearrange("(t p) h -> p t h", p=P)).then_inc(w_loaded[n], DMA)

            def store_half(r, u, half):
                s, b = u % SLOTS, graph(r, u)
                sp.wait_ge(y_normed, 2 * b + half + 1)
                sp.dma_start(out_dram[b, half], y[s][:, half * PER_BANK:(half + 1) * PER_BANK]
                             ).then_inc(stored[s], DMA)

            def step(r, u, load):
                b = graph(r, u)
                if load:
                    sp.wait_ge(adjT_hi_ready, MT * (b + 1))
                    load_adj(r, u + SLOTS)
                for half in range(2):
                    store_half(r, u, half)
                sp.wait_ge(stored[u % SLOTS], 2 * dma_count(r, u))
                if load:
                    load_x(r, u + SLOTS)

            load_x(0, 0)
            for t in range(MT):
                sp.dma_start(adj_raw[0][:, t], adj_dram[0, t]).then_inc(tile_loaded[t], DMA)
            load_w(0, W1)
            load_w(1, W2)
            load_w(2, W3)
            sp.dma_start(adj_raw[1][:], adj_dram[1].rearrange("t p m -> p t m")).then_inc(second_loaded, DMA)
            load_x(0, 1)
            load_adj(0, 2)
            load_x(0, 2)
            with sp.Fori(0, ROUNDS) as r:
                for u in range(SLOTS):
                    step(r, u, True)
            for b in range(LOOPED, B):
                step(0, b, b + SLOTS < B)

        @block.gpsimd
        def _(pool):
            def lo_of_x(r, u):
                s, c = u % SLOTS, graph(r, u)
                pool.wait_ge(x_hi_ready, c + 1)
                nc.gpsimd.tensor_tensor(x_lo[:], x_rows[s][:], x_hi[:].bitcast(F32), ALU.subtract
                                        ).then_inc(x_lo_ready, 1)

            def bias_x(r, u):
                s, b = u % SLOTS, graph(r, u)
                pool.wait_ge(x_lo_ready, b + 1)
                nc.gpsimd.tensor_tensor(x_rows[s][:], x_rows[s][:], b3_rows[:], ALU.add).then_inc(x_biased, 1)

            def root(r, u, half):
                b = graph(r, u)
                cols = slice(half * PER_BANK, (half + 1) * PER_BANK)
                pool.wait_ge(var_ready, 2 * b + half + 1)
                nc.gpsimd.tensor_tensor(rstd[:, cols], var_eps[:, cols], minus_half[:], ALU.pow
                                        ).then_inc(rstd_ready, 1)

            def step(r, u, split):
                bias_x(r, u)
                if split:
                    lo_of_x(r, u + 2)
                for half in range(2):
                    root(r, u, half)

            nc.gpsimd.memset(ident[:], 0.0).then_inc(const_set, 1)
            nc.gpsimd.memset(minus_half[:], -0.5).then_inc(const_set, 1)
            pool.wait_ge(const_set, 2)
            nc.gpsimd.affine_select(out=ident[:], in_=ident[:], compare_op=ALU.not_equal, fill=1.0, base=0,
                                    pattern=[[-1, P]], channel_multiplier=1).then_inc(ident_ready, 1)
            lo_of_x(0, 0)
            pool.wait_ge(bias_loaded, 3 * DMA)
            lo_of_x(0, 1)
            with pool.Fori(0, ROUNDS) as r:
                for u in range(SLOTS):
                    step(r, u, True)
            for b in range(LOOPED, B):
                step(0, b, b + 2 < B)

        @block.tensor
        def _(pe):
            def three_passes(acc, st_hi, st_lo, mv_hi, mv_lo, start, stop):
                nc.tensor.matmul(acc, st_hi, mv_hi, start=start, stop=False)
                nc.tensor.matmul(acc, st_hi, mv_lo, start=False, stop=False)
                return nc.tensor.matmul(acc, st_lo, mv_hi, start=False, stop=stop)

            def turn_first():
                for j in range(MT):
                    pe.wait_ge(tile_loaded[j], DMA)
                    for k in range(MT):
                        mm = nc.tensor.transpose(first_turned[k][:, j * P:(j + 1) * P],
                                                 adj_raw[0][:, j, k * P:(k + 1) * P], ident[:])
                        if j == MT - 1:
                            mm.then_inc(turn_done, 1)

            def turn_second(k):
                pe.wait_ge(second_loaded, DMA)
                pe.wait_ge(adjT_lo_ready, MT + k - 1)
                for j in range(MT):
                    mm = nc.tensor.transpose(turned[k % 2][:, j * P:(j + 1) * P],
                                             adj_raw[1][:, j, k * P:(k + 1) * P], ident[:])
                mm.then_inc(turn_done, 1)

            def aggregate(r, u):
                s, c = u % SLOTS, graph(r, u)
                pe.wait_ge(x_lo_ready, c + 1)
                for k in range(MT):
                    pe.wait_ge(adjT_lo_ready, MT * c + k + 1)
                    for f in range(FT):
                        cols = slice(f * P, (f + 1) * P)
                        mm = three_passes(acc_a[f][:], x_hi[:, k, cols], x_lo[:, k, cols],
                                          adjT_hi[s][:, k], adjT_lo[s][:, k], k == 0, k == MT - 1)
                        if k == MT - 1:
                            mm.then_inc(ax_done, 1)

            def dense1(r, u):
                c = graph(r, u)
                for h in range(FT):
                    cols = slice(h * P, (h + 1) * P)
                    for k in range(FT):
                        if h == 0:
                            pe.wait_ge(ax_lo_ready, 2 * c + k + 1)
                        mm = three_passes(acc_c[h][:], w_hi[:, 0, k, cols], w_lo[:, 0, k, cols],
                                          axT_hi[:, k], axT_lo[:, k], k == 0, k == FT - 1)
                    mm.then_inc(h1_done, 1)

            def support(acc, hT_hi, hT_lo, layer, lo_ready, done, c):
                for m in range(MT):
                    cols = slice(m * P, (m + 1) * P)
                    part = slice(m % PER_BANK * F, (m % PER_BANK + 1) * F)
                    for k in range(FT):
                        if m == 0:
                            pe.wait_ge(lo_ready, 2 * c + k + 1)
                        mm = three_passes(acc[m // PER_BANK][:, part], hT_hi[:, k, cols], hT_lo[:, k, cols],
                                          w_hi[:, layer, k], w_lo[:, layer, k], k == 0, k == FT - 1)
                    if m % PER_BANK == PER_BANK - 1:
                        mm.then_inc(done, 1)

            def support2(r, u):
                support(acc_b, h1T_hi, h1T_lo, 1, h1_lo_ready, s2_done, graph(r, u))

            def support3(r, u):
                support(acc_a, h2T_hi, h2T_lo, 2, h2_lo_ready, s3_done, graph(r, u))

            def hidden2(r, u):
                s, b = u % SLOTS, graph(r, u)
                for h in range(FT):
                    cols = slice(h * P, (h + 1) * P)
                    for k in range(MT):
                        if h == 0 and k % PER_BANK == 0:
                            pe.wait_ge(s2_lo_ready, 2 * b + (k // PER_BANK) + 1 if k else 2 * b + 2)
                        mm = three_passes(acc_b[h][:], s2_hi[:, k, cols], s2_lo[:, k, cols],
                                          adjT_hi[s][:, k], adjT_lo[s][:, k], k == 0, k == MT - 1)
                    mm.then_inc(h2_done, 1)

            def output(r, u):
                s, b = u % SLOTS, graph(r, u)
                for n in range(MT):
                    cols = slice(n * P, (n + 1) * P)
                    part = slice(n % PER_BANK * F, (n % PER_BANK + 1) * F)
                    for k in range(MT):
                        if n == 0 and k % PER_BANK == 0:
                            pe.wait_ge(s3_lo_ready, 2 * b + k // PER_BANK + 1)
                        mm = three_passes(acc_c[n // PER_BANK][:, part], adjT_hi[s][:, k, cols],
                                          adjT_lo[s][:, k, cols], s3_hi[:, k], s3_lo[:, k], k == 0, k == MT - 1)
                    if n % PER_BANK == PER_BANK - 1:
                        mm.then_inc(y_done, 1)

            def step(r, u, ahead):
                if ahead:
                    aggregate(r, u + 1)
                hidden2(r, u)
                if ahead:
                    dense1(r, u + 1)
                support3(r, u)
                if ahead:
                    support2(r, u + 1)
                output(r, u)

            pe.wait_ge(ident_ready, 1)
            turn_first()
            aggregate(0, 0)
            turn_second(0)
            turn_second(1)
            pe.wait_ge(w_lo_ready, 1)
            dense1(0, 0)
            pe.wait_ge(w_lo_ready, 3)
            turn_second(2)
            support2(0, 0)
            turn_second(3)
            with pe.Fori(0, ROUNDS) as r:
                for u in range(SLOTS):
                    step(r, u, True)
            for b in range(LOOPED, B):
                step(0, b, b + 1 < B)

        @block.scalar
        def _(act):
            def hi_of_turn(r, u, k):
                if isinstance(r, int) and u < 2:
                    source = (first_turned if u == 0 else turned * 2)[k]
                    act.wait_ge(turn_done, MT * u + k + 1)
                else:
                    source = turned[k % 2]
                    act.wait_ge(squares_turned, MT * graph(r, u - 2) + k + 1)
                nc.scalar.activation(adjT_hi[u % SLOTS][:, k], source[:], ACT.Copy).then_inc(adjT_hi_ready, 1)

            def hi_of(hi, acc, done, ready, c):
                for half in range(2):
                    act.wait_ge(done, 2 * c + half + 1)
                    nc.scalar.activation(hi[half], acc[half][:], ACT.Copy).then_inc(ready, 1)

            def relu_hi_of(hi, acc, bias, done, relu_done, ready, c):
                for half in range(2):
                    act.wait_ge(done, 2 * c + half + 1)
                    nc.scalar.activation(acc[half][:], acc[half][:], ACT.Relu, bias=bias[:, half:half + 1]
                                         ).then_inc(relu_done, 1)
                    act.wait_ge(relu_done, 2 * c + half + 1)
                    nc.scalar.activation(hi[half], acc[half][:], ACT.Copy).then_inc(ready, 1)

            rows = lambda t: [t[:, k] for k in range(FT)]
            nodes = lambda t: [t[:, h * PER_BANK:(h + 1) * PER_BANK].rearrange("p t f -> p (t f)")
                               for h in range(HALVES)]

            def ax(c):
                hi_of(rows(axT_hi), acc_a, ax_done, ax_hi_ready, c)

            def h1(c):
                relu_hi_of(rows(h1T_hi), acc_c, b1_col, h1_done, h1_relu_done, h1_hi_ready, c)

            def s2(c):
                hi_of(nodes(s2_hi), acc_b, s2_done, s2_hi_ready, c)

            def h2(c):
                relu_hi_of(rows(h2T_hi), acc_b, b2_col, h2_done, h2_relu_done, h2_hi_ready, c)

            def s3(c):
                hi_of(nodes(s3_hi), acc_a, s3_done, s3_hi_ready, c)

            def step(r, u, ahead, turning):
                b = graph(r, u)
                if ahead:
                    ax(b + 1)
                if turning:
                    hi_of_turn(r, u + 2, 0)
                    hi_of_turn(r, u + 2, 1)
                h2(b)
                if ahead:
                    h1(b + 1)
                s3(b)
                if ahead:
                    s2(b + 1)
                if turning:
                    hi_of_turn(r, u + 2, 2)
                    hi_of_turn(r, u + 2, 3)

            act.dma_start(b1_col[:], b1.rearrange("(t p) -> p t", p=P), allow_slow_non_contiguous=True
                          ).then_inc(bias_loaded, DMA)
            act.dma_start(b2_col[:], b2.rearrange("(t p) -> p t", p=P), allow_slow_non_contiguous=True
                          ).then_inc(bias_loaded, DMA)
            act.dma_start(b3_rows[:], b3.partition_broadcast(P).unsqueeze(1).broadcast_to([P, MT, F])
                          ).then_inc(bias_loaded, DMA)
            for k in range(MT):
                hi_of_turn(0, 0, k)
            for n in range(3):
                act.wait_ge(w_loaded[n], DMA)
                nc.scalar.activation(w_hi[:, n], w_raw[:, n], ACT.Copy).then_inc(w_hi_ready, 1)
            act.wait_ge(bias_loaded, 3 * DMA)
            ax(0)
            hi_of_turn(0, 1, 0)
            hi_of_turn(0, 1, 1)
            h1(0)
            hi_of_turn(0, 1, 2)
            s2(0)
            hi_of_turn(0, 1, 3)
            with act.Fori(0, ROUNDS) as r:
                for u in range(SLOTS):
                    step(r, u, True, True)
            for b in range(LOOPED, B):
                step(0, b, b + 1 < B, b + 2 < B)

        @block.vector
        def _(dve):
            def turn(r, u, k):
                s = u % SLOTS
                if k == 0:
                    dve.wait_ge(adj_loaded[s], QUADS * dma_count(r, u - 2))
                nc.vector.transpose(turned[k % 2][:], adj_raw[s][:, k]).then_inc(squares_turned, 1)

            def lo_of_turn(r, u, k):
                s, c = u % SLOTS, graph(r, u)
                source = first_turned[k] if isinstance(c, int) and c == 0 else turned[k % 2]
                dve.wait_ge(adjT_hi_ready, MT * c + k + 1)
                nc.vector.tensor_tensor(adjT_lo[s][:, k], source[:], adjT_hi[s][:, k].bitcast(F32),
                                        ALU.subtract).then_inc(adjT_lo_ready, 1)

            def turn_pair(r, u, k):
                for each in (turn, lo_of_turn):
                    each(r, u, k)
                    each(r, u, k + 1)

            def lo_of(lo, acc, hi, hi_ready, lo_ready, c):
                for half in range(2):
                    dve.wait_ge(hi_ready, 2 * c + half + 1)
                    nc.vector.tensor_tensor(lo[half], acc[half][:], hi[half].bitcast(F32), ALU.subtract
                                            ).then_inc(lo_ready, 1)

            rows = lambda t: [t[:, k] for k in range(FT)]
            nodes = lambda t: [t[:, h * PER_BANK:(h + 1) * PER_BANK].rearrange("p t f -> p (t f)")
                               for h in range(HALVES)]

            def ax(c):
                lo_of(rows(axT_lo), acc_a, rows(axT_hi), ax_hi_ready, ax_lo_ready, c)

            def h1(c):
                lo_of(rows(h1T_lo), acc_c, rows(h1T_hi), h1_hi_ready, h1_lo_ready, c)

            def s2(c):
                lo_of(nodes(s2_lo), acc_b, nodes(s2_hi), s2_hi_ready, s2_lo_ready, c)

            def h2(c):
                lo_of(rows(h2T_lo), acc_b, rows(h2T_hi), h2_hi_ready, h2_lo_ready, c)

            def s3(c):
                lo_of(nodes(s3_lo), acc_a, nodes(s3_hi), s3_hi_ready, s3_lo_ready, c)

            def hi_of_x(r, u):
                s, c = u % SLOTS, graph(r, u)
                dve.wait_ge(x_loaded[s], dma_count(r, u))
                if u > 0:
                    dve.wait_ge(ax_done, 2 * c)
                nc.vector.tensor_copy(x_hi[:], x_rows[s][:]).then_inc(x_hi_ready, 1)

            def norm(r, u):
                s, b = u % SLOTS, graph(r, u)
                dve.wait_ge(x_biased, b + 1)
                if isinstance(b, int) and b + 1 == B:
                    dve.wait_ge(stored[s], 2 * dma_count(r, u - SLOTS))
                for half in range(2):
                    mine = slice(half * PER_BANK, (half + 1) * PER_BANK)
                    dve.wait_ge(y_done, 2 * b + half + 1)
                    nc.vector.tensor_tensor(y[s][:, mine].rearrange("p t f -> p (t f)"), acc_c[half][:],
                                            x_rows[s][:, mine].rearrange("p t f -> p (t f)"), ALU.add
                                            ).then_inc(y_added, 1)
                    dve.wait_ge(y_added, 2 * b + half + 1)
                    for n in range(mine.start, mine.stop):
                        nc.vector.bn_stats(stats[:, n], y[s][:, n]).then_inc(stats_done, 1)
                    dve.wait_ge(stats_done, MT * b + mine.stop)
                    even, odd = stats[:, mine, 1], stats[:, mine, 4]
                    nc.vector.tensor_tensor(mean_sum[:, mine], even, odd, ALU.add).then_inc(pair_done, 1)
                    nc.vector.tensor_tensor(mean_gap[:, mine], even, odd, ALU.subtract).then_inc(pair_done, 1)
                    nc.vector.scalar_tensor_tensor(squares[:, mine], stats[:, mine, 2], F * EPS,
                                                   stats[:, mine, 5], ALU.add, ALU.add).then_inc(pair_done, 1)
                    dve.wait_ge(pair_done, 6 * b + 3 * half + 3)
                    nc.vector.scalar_tensor_tensor(gap_square[:, mine], mean_gap[:, mine], 0.25,
                                                   mean_gap[:, mine], ALU.mult, ALU.mult).then_inc(gap_done, 1)
                    nc.vector.tensor_scalar(mean[:, mine], mean_sum[:, mine], 0.5, None, ALU.mult
                                            ).then_inc(mean_ready, 1)
                    dve.wait_ge(gap_done, 2 * b + half + 1)
                    nc.vector.scalar_tensor_tensor(var_eps[:, mine], squares[:, mine], 1.0 / F,
                                                   gap_square[:, mine], ALU.mult, ALU.add
                                                   ).then_inc(var_ready, 1)
                for half in range(2):
                    dve.wait_ge(mean_ready, 2 * b + half + 1)
                    dve.wait_ge(rstd_ready, 2 * b + half + 1)
                    for n in range(half * PER_BANK, (half + 1) * PER_BANK):
                        last = nc.vector.tensor_scalar(y[s][:, n], y[s][:, n], mean[:, n:n + 1],
                                                       rstd[:, n:n + 1], ALU.subtract, ALU.mult)
                    last.then_inc(y_normed, 1)

            def step(r, u, ahead, turning):
                b = graph(r, u)
                if ahead:
                    ax(b + 1)
                if turning:
                    turn_pair(r, u + 2, 0)
                h2(b)
                if ahead:
                    h1(b + 1)
                if turning:
                    hi_of_x(r, u + 2)
                s3(b)
                if ahead:
                    s2(b + 1)
                if turning:
                    turn_pair(r, u + 2, 2)
                norm(r, u)

            hi_of_x(0, 0)
            for k in range(MT):
                lo_of_turn(0, 0, k)
            for n in range(3):
                dve.wait_ge(w_hi_ready, n + 1)
                nc.vector.tensor_tensor(w_lo[:, n], w_raw[:, n], w_hi[:, n].bitcast(F32), ALU.subtract
                                        ).then_inc(w_lo_ready, 1)
            ax(0)
            lo_of_turn(0, 1, 0)
            lo_of_turn(0, 1, 1)
            hi_of_x(0, 1)
            h1(0)
            lo_of_turn(0, 1, 2)
            s2(0)
            lo_of_turn(0, 1, 3)
            with dve.Fori(0, ROUNDS) as r:
                for u in range(SLOTS):
                    step(r, u, True, True)
            for b in range(LOOPED, B):
                step(0, b, b + 1 < B, b + 2 < B)


def kernel(x, adj, L0_gnn_W1, L0_gnn_b1, L0_gnn_W2, L0_gnn_b2, L0_gnn_W3, L0_gnn_b3):
    import numpy as np
    import concourse.bacc as bacc
    from concourse.bass_utils import run_bass_kernel_spmd

    nc = bacc.Bacc("TRN2", target_bir_lowering=False, num_devices=1)
    inputs = {"x": x, "adj": adj, "W1": L0_gnn_W1, "b1": L0_gnn_b1, "W2": L0_gnn_W2, "b2": L0_gnn_b2,
              "W3": L0_gnn_W3, "b3": L0_gnn_b3}
    arrays, args = {}, []
    for name, value in inputs.items():
        a = np.ascontiguousarray(value)
        arrays[f"in_{name}"] = a
        args.append(nc.dram_tensor(f"in_{name}", a.shape, mybir.dt.from_np(a.dtype), kind="ExternalInput").ap())
    args.append(nc.dram_tensor("out_y", x.shape, F32, kind="ExternalOutput").ap())
    gcn_resnorm(nc, *args)
    result = run_bass_kernel_spmd(nc, [arrays], core_ids=[0])
    return result.results[0]["out_y"]
```

```python
from contextlib import ExitStack

import concourse.bass as bass
from concourse import mybir

P = 128
SLOTS = 3
SQ = 32
BANK = 512
EPS = 1e-5
WARM_UP = 5
DMA = 16

ALU = mybir.AluOpType
ACT = mybir.ActivationFunctionType
ENGINE = mybir.EngineType
F32 = mybir.dt.float32
F32R = mybir.dt.float32r


def gcn_resnorm(nc, x, adj, W1, b1, W2, b2, W3, b3, out):
    B, N, F = x.shape
    MT = N // P
    FT = F // P
    HALVES = MT * F // BANK
    PER_BANK = MT // HALVES
    assert N == BANK and FT == HALVES == 2 and MT == 4
    ROUNDS = (B - 2) // SLOTS
    LOOPED = ROUNDS * SLOTS

    x_dram = x.rearrange("b (t p) f -> b p t f", p=P)
    adj_dram = adj.rearrange("b (t p) m -> b t p m", p=P)
    QUADS = P // SQ
    squares_dram = adj.rearrange("b (n j) (k a i) -> b a j k n i", j=SQ, a=QUADS, i=SQ)
    out_dram = out.rearrange("b (t p) f -> b p t f", p=P)

    with ExitStack() as ctx:
        def sb(name, shape, dt=F32):
            return ctx.enter_context(nc.sbuf_tensor(name, shape, dt))

        def bank(name):
            return ctx.enter_context(nc.psum_tensor(name, [P, BANK], F32))

        def sem(name):
            return ctx.enter_context(nc.semaphore(name))

        ident = sb("ident", [P, P])
        zeros = sb("zeros", [P, BANK], mybir.dt.bfloat16)
        w_raw = sb("w_raw", [P, 3, FT, F])
        w_hi = sb("w_hi", [P, 3, FT, F], F32R)
        w_lo = sb("w_lo", [P, 3, FT, F], F32R)
        b1_col = sb("b1_col", [P, FT])
        b2_col = sb("b2_col", [P, FT])
        b3_rows = sb("b3_rows", [P, MT, F])
        minus_half = sb("minus_half", [P, PER_BANK])
        adj_raw = [sb(f"adj_raw{s}", [P, MT, N]) for s in range(SLOTS)]
        adjT_hi = [sb(f"adjT_hi{s}", [P, MT, N], F32R) for s in range(SLOTS)]
        adjT_lo = [sb(f"adjT_lo{s}", [P, MT, N], F32R) for s in range(SLOTS)]
        x_rows = [sb(f"x_rows{s}", [P, MT, F]) for s in range(SLOTS)]
        x_hi = sb("x_hi", [P, MT, F], F32R)
        x_lo = sb("x_lo", [P, MT, F], F32R)
        axT_hi = sb("axT_hi", [P, FT, N], F32R)
        axT_lo = sb("axT_lo", [P, FT, N], F32R)
        h1T_hi = sb("h1T_hi", [P, FT, N], F32R)
        h1T_lo = sb("h1T_lo", [P, FT, N], F32R)
        h2T_hi = sb("h2T_hi", [P, FT, N], F32R)
        h2T_lo = sb("h2T_lo", [P, FT, N], F32R)
        s2_hi = sb("s2_hi", [P, MT, F], F32R)
        s2_lo = sb("s2_lo", [P, MT, F], F32R)
        s3_hi = sb("s3_hi", [P, MT, F], F32R)
        s3_lo = sb("s3_lo", [P, MT, F], F32R)
        y = [sb(f"y{s}", [P, MT, F]) for s in range(SLOTS)]
        stats = sb("stats", [P, MT, 6])
        mean_sum = sb("mean_sum", [P, MT])
        mean_gap = sb("mean_gap", [P, MT])
        squares = sb("squares", [P, MT])
        gap_square = sb("gap_square", [P, MT])
        mean = sb("mean", [P, MT])
        mean_var = sb("mean_var", [P, MT, 2])
        var_eps = sb("var_eps", [P, MT])
        rstd = sb("rstd", [P, MT])

        turned = [bank(f"turned{k}") for k in range(2)]
        acc_a = [bank(f"acc_a{k}") for k in range(2)]
        acc_b = [bank(f"acc_b{k}") for k in range(2)]
        acc_c = [bank(f"acc_c{k}") for k in range(2)]
        first_turned = turned + acc_b
        HALF_PARTS = [(i, range(i * PER_BANK, (i + 1) * PER_BANK), acc_c[i]) for i in range(HALVES)]
        LAST_PARTS = [(i, range(i, i + 1), acc) for i, acc in enumerate([acc_c[0], turned[0], turned[1], acc_c[1]])]

        tile_loaded = [sem(f"tile_loaded{t}") for t in range(MT)]
        second_loaded = sem("second_loaded")
        adj_loaded = [sem(f"adj_loaded{s}") for s in range(SLOTS)]
        x_loaded = [sem(f"x_loaded{s}") for s in range(SLOTS)]
        x_tile_loaded = [sem(f"x_tile_loaded{t}") for t in range(MT - 1)]
        w_loaded = [sem(f"w_loaded{n}") for n in range(3)]
        bias_loaded, b3_loaded = sem("bias_loaded"), sem("b3_loaded")
        stored = [sem(f"stored{s}") for s in range(SLOTS)]
        const_set = sem("const_set")
        ident_ready, zeros_ready = sem("ident_ready"), sem("zeros_ready")
        w_hi_ready, w_lo_ready = sem("w_hi_ready"), sem("w_lo_ready")
        x_hi_ready, x_lo_ready = sem("x_hi_ready"), sem("x_lo_ready")
        x_tile_hi_ready, x_tile_lo_ready = sem("x_tile_hi_ready"), sem("x_tile_lo_ready")
        x_biased = sem("x_biased")
        squares_turned = sem("squares_turned")
        turn_done = sem("turn_done")
        ax_done, h1_done, s2_done = sem("ax_done"), sem("h1_done"), sem("s2_done")
        h2_done, s3_done, y_done = sem("h2_done"), sem("s3_done"), sem("y_done")
        adjT_hi_ready, adjT_lo_ready = sem("adjT_hi_ready"), sem("adjT_lo_ready")
        ax_hi_ready, ax_lo_ready = sem("ax_hi_ready"), sem("ax_lo_ready")
        h1_hi_ready, h1_lo_ready = sem("h1_hi_ready"), sem("h1_lo_ready")
        s2_hi_ready, s2_lo_ready = sem("s2_hi_ready"), sem("s2_lo_ready")
        h2_hi_ready, h2_lo_ready = sem("h2_hi_ready"), sem("h2_lo_ready")
        s3_hi_ready, s3_lo_ready = sem("s3_hi_ready"), sem("s3_lo_ready")
        h1_relu_done, h2_relu_done = sem("h1_relu_done"), sem("h2_relu_done")
        y_added = sem("y_added")
        stats_done, pair_done = sem("stats_done"), sem("pair_done")
        gap_done, mean_ready, var_ready = sem("gap_done"), sem("mean_ready"), sem("var_ready")
        rstd_ready, y_normed = sem("rstd_ready"), sem("y_normed")

        def graph(r, u):
            return r * SLOTS + u

        def dma_count(r, u):
            return DMA * (r + u // SLOTS + 1)

        def rounds(engine):
            return nc.Fori(0, ROUNDS, engines=(engine,), hint_back_edge=True)

        block = ctx.enter_context(nc.Block())

        @block.sync
        def _(sp):
            def load_adj(r, u):
                s, c = u % SLOTS, graph(r, u)
                for a in range(QUADS):
                    part = adj_raw[s][a * SQ:(a + 1) * SQ].rearrange("j k (n i) -> j k n i", i=SQ)
                    sp.dma_start(part, squares_dram[c, a]).then_inc(adj_loaded[s], DMA)

            def load_x(r, u):
                sp.dma_start(x_rows[u % SLOTS][:], x_dram[graph(r, u)]).then_inc(x_loaded[u % SLOTS], DMA)

            def load_w(n, w):
                sp.dma_start(w_raw[:, n], w.rearrange("(t p) h -> p t h", p=P)).then_inc(w_loaded[n], DMA)

            def store(r, u, parts):
                s, b = u % SLOTS, graph(r, u)
                for i, tiles, _ in parts:
                    sp.wait_ge(y_normed, 2 * b + i + 1)
                    mine = slice(tiles.start, tiles.stop)
                    sp.dma_start(out_dram[b, :, mine], y[s][:, mine]).then_inc(stored[s], DMA)

            def step(r, u, load):
                b = graph(r, u)
                if load:
                    sp.wait_ge(adjT_hi_ready, MT * (b + 1))
                    load_adj(r, u + SLOTS)
                store(r, u, HALF_PARTS)
                sp.wait_ge(stored[u % SLOTS], 2 * dma_count(r, u))
                if load:
                    load_x(r, u + SLOTS)

            for t in range(MT):
                sp.dma_start(adj_raw[0][:, t], adj_dram[0, t]).then_inc(tile_loaded[t], DMA)
            for t, loaded in enumerate(x_tile_loaded + x_loaded[:1]):
                sp.dma_start(x_rows[0][:, t], x_dram[0, :, t]).then_inc(loaded, DMA)
            load_w(0, W1)
            for column, bias in ((b1_col, b1), (b2_col, b2)):
                sp.dma_start(column[:], bias.rearrange("(t p) -> p t", p=P), allow_slow_non_contiguous=True
                             ).then_inc(bias_loaded, DMA)
            load_w(1, W2)
            load_w(2, W3)
            sp.dma_start(adj_raw[1][:], adj_dram[1].rearrange("t p m -> p t m")).then_inc(second_loaded, DMA)
            load_x(0, 1)
            sp.dma_start(b3_rows[:], b3.partition_broadcast(P).unsqueeze(1).broadcast_to([P, MT, F])
                         ).then_inc(b3_loaded, DMA)
            load_adj(0, 2)
            load_x(0, 2)
            with rounds(ENGINE.SP) as r:
                for u in range(SLOTS):
                    step(r, u, True)
            for b in range(LOOPED, B - 1):
                step(0, b, b + SLOTS < B)
            store(0, B - 1, [(1, range(2), None), LAST_PARTS[2]])
            sp.wait_ge(stored[(B - 1) % SLOTS], 2 * dma_count(0, B - 1 - SLOTS) + 3 * DMA)

        @block.gpsimd
        def _(pool):
            def lo_of_x(r, u):
                s, c = u % SLOTS, graph(r, u)
                pool.wait_ge(x_hi_ready, c + 1)
                nc.gpsimd.tensor_tensor(x_lo[:], x_rows[s][:], x_hi[:].bitcast(F32), ALU.subtract
                                        ).then_inc(x_lo_ready, 1)

            def bias_x(r, u):
                s, b = u % SLOTS, graph(r, u)
                pool.wait_ge(x_lo_ready, b + 1)
                nc.gpsimd.tensor_tensor(x_rows[s][:], x_rows[s][:], b3_rows[:], ALU.add).then_inc(x_biased, 1)

            def root(r, u, parts):
                b = graph(r, u)
                for i, tiles, _ in parts:
                    mine = slice(tiles.start, tiles.stop)
                    pool.wait_ge(var_ready, 2 * b + i + 1)
                    nc.gpsimd.tensor_tensor(rstd[:, mine], var_eps[:, mine], minus_half[:, :len(tiles)], ALU.pow
                                            ).then_inc(rstd_ready, 1)

            def step(r, u, split):
                bias_x(r, u)
                if split:
                    lo_of_x(r, u + 2)
                root(r, u, HALF_PARTS)

            nc.gpsimd.memset(ident[:], 0.0).then_inc(const_set, 1)
            nc.gpsimd.memset(minus_half[:], -0.5).then_inc(const_set, 1)
            pool.wait_ge(const_set, 2)
            nc.gpsimd.affine_select(out=ident[:], in_=ident[:], compare_op=ALU.not_equal, fill=1.0, base=0,
                                    pattern=[[-1, P]], channel_multiplier=1).then_inc(ident_ready, 1)
            for t in range(MT):
                if t < MT - 1:
                    pool.wait_ge(x_tile_hi_ready, t + 1)
                else:
                    pool.wait_ge(x_hi_ready, 1)
                nc.gpsimd.tensor_tensor(x_lo[:, t], x_rows[0][:, t], x_hi[:, t].bitcast(F32), ALU.subtract
                                        ).then_inc(x_tile_lo_ready if t < MT - 1 else x_lo_ready, 1)
            pool.wait_ge(b3_loaded, DMA)
            lo_of_x(0, 1)
            with rounds(ENGINE.Pool) as r:
                for u in range(SLOTS):
                    step(r, u, True)
            for b in range(LOOPED, B - 1):
                step(0, b, b + 2 < B)
            bias_x(0, B - 1)
            root(0, B - 1, LAST_PARTS)

        @block.tensor
        def _(pe):
            def three_passes(acc, st_hi, st_lo, mv_hi, mv_lo, start, stop):
                nc.tensor.matmul(acc, st_hi, mv_hi, start=start, stop=False)
                nc.tensor.matmul(acc, st_hi, mv_lo, start=False, stop=False)
                return nc.tensor.matmul(acc, st_lo, mv_hi, start=False, stop=stop)

            def turn_first():
                for j in range(MT):
                    pe.wait_ge(tile_loaded[j], DMA)
                    for k in range(MT):
                        mm = nc.tensor.transpose(first_turned[k][:, j * P:(j + 1) * P],
                                                 adj_raw[0][:, j, k * P:(k + 1) * P], ident[:])
                        if j == MT - 1:
                            mm.then_inc(turn_done, 1)

            def turn_second(k):
                pe.wait_ge(second_loaded, DMA)
                pe.wait_ge(adjT_lo_ready, MT + k - 1)
                for j in range(MT):
                    mm = nc.tensor.transpose(turned[k % 2][:, j * P:(j + 1) * P],
                                             adj_raw[1][:, j, k * P:(k + 1) * P], ident[:])
                mm.then_inc(turn_done, 1)

            def aggregate(r, u):
                s, c = u % SLOTS, graph(r, u)
                first_graph = isinstance(r, int) and c == 0
                if not first_graph:
                    pe.wait_ge(x_lo_ready, c + 1)
                for k in range(MT):
                    if first_graph and k < MT - 1:
                        pe.wait_ge(x_tile_lo_ready, k + 1)
                    elif first_graph:
                        pe.wait_ge(x_lo_ready, 1)
                    x_k = [(x_hi[:, k, f * P:(f + 1) * P], x_lo[:, k, f * P:(f + 1) * P]) for f in range(FT)]
                    pe.wait_ge(adjT_hi_ready, MT * c + k + 1)
                    if k < MT - 1:
                        for acc, (hi, lo) in zip(acc_a, x_k):
                            nc.tensor.matmul(acc[:], hi, adjT_hi[s][:, k], start=k == 0, stop=False)
                            nc.tensor.matmul(acc[:], lo, adjT_hi[s][:, k], start=False, stop=False)
                        pe.wait_ge(adjT_lo_ready, MT * c + k + 1)
                        for acc, (hi, lo) in zip(acc_a, x_k):
                            nc.tensor.matmul(acc[:], hi, adjT_lo[s][:, k], start=False, stop=False)
                    else:
                        pe.wait_ge(adjT_lo_ready, MT * c + k + 1)
                        for acc, (hi, lo) in zip(acc_a, x_k):
                            three_passes(acc[:], hi, lo, adjT_hi[s][:, k], adjT_lo[s][:, k], False, True
                                         ).then_inc(ax_done, 1)

            def dense1(r, u):
                c = graph(r, u)
                for h in range(FT):
                    cols = slice(h * P, (h + 1) * P)
                    for k in range(FT):
                        if h == 0:
                            pe.wait_ge(ax_lo_ready, 2 * c + k + 1)
                        mm = three_passes(acc_c[h][:], w_hi[:, 0, k, cols], w_lo[:, 0, k, cols],
                                          axT_hi[:, k], axT_lo[:, k], k == 0, k == FT - 1)
                    mm.then_inc(h1_done, 1)

            def support(acc, hT_hi, hT_lo, layer, lo_ready, done, c, groups):
                for group in groups:
                    for k in range(FT):
                        if group is groups[0]:
                            pe.wait_ge(lo_ready, 2 * c + k + 1)
                        for m in group:
                            cols = slice(m * P, (m + 1) * P)
                            half, at = m // PER_BANK, m % PER_BANK * F
                            mm = three_passes(acc[half][:, at:at + F], hT_hi[:, k, cols], hT_lo[:, k, cols],
                                              w_hi[:, layer, k], w_lo[:, layer, k], k == 0, k == FT - 1)
                            if k == FT - 1 and m % PER_BANK == PER_BANK - 1:
                                mm.then_inc(done, 1)

            def support2(r, u):
                support(acc_b, h1T_hi, h1T_lo, 1, h1_lo_ready, s2_done, graph(r, u), SPREAD)

            def support3(r, u, groups):
                support(acc_a, h2T_hi, h2T_lo, 2, h2_lo_ready, s3_done, graph(r, u), groups)

            def hidden2(r, u):
                s, b = u % SLOTS, graph(r, u)
                pe.wait_ge(s2_lo_ready, 2 * b + 2)
                for h in range(FT):
                    cols = slice(h * P, (h + 1) * P)
                    for k in range(MT):
                        mm = three_passes(acc_b[h][:], s2_hi[:, k, cols], s2_lo[:, k, cols],
                                          adjT_hi[s][:, k], adjT_lo[s][:, k], k == 0, k == MT - 1)
                    mm.then_inc(h2_done, 1)

            SPREAD = [range(i, MT, PER_BANK) for i in range(PER_BANK)]
            SINGLE = [[m] for m in range(MT)]

            def output(r, u, parts):
                s, b = u % SLOTS, graph(r, u)
                pe.wait_ge(s3_lo_ready, 2 * b + 2)
                for _, tiles, acc in parts:
                    for n in tiles:
                        cols = slice(n * P, (n + 1) * P)
                        at = (n - tiles[0]) * F
                        for k in range(MT):
                            mm = three_passes(acc[:, at:at + F], adjT_hi[s][:, k, cols], adjT_lo[s][:, k, cols],
                                              s3_hi[:, k], s3_lo[:, k], k == 0, k == MT - 1)
                    mm.then_inc(y_done, 1)

            def output_last():
                s = (B - 1) % SLOTS
                for ks, tiles in ((range(PER_BANK), range(2)), (range(PER_BANK, MT), range(2)),
                                  (range(MT), range(2, 3)), (range(MT), range(3, 4))):
                    pe.wait_ge(s3_lo_ready, 2 * (B - 1) + ks[-1] // PER_BANK + 1)
                    for n in tiles:
                        cols = slice(n * P, (n + 1) * P)
                        for k in ks:
                            mm = three_passes(LAST_PARTS[n][2][:, :F], adjT_hi[s][:, k, cols],
                                              adjT_lo[s][:, k, cols], s3_hi[:, k], s3_lo[:, k],
                                              k == 0, k == MT - 1)
                        if ks[-1] == MT - 1:
                            mm.then_inc(y_done, 1)

            def step(r, u):
                aggregate(r, u + 1)
                hidden2(r, u)
                dense1(r, u + 1)
                support3(r, u, SPREAD)
                support2(r, u + 1)
                output(r, u, HALF_PARTS)

            pe.wait_ge(zeros_ready, 1)
            for _ in range(WARM_UP):
                nc.tensor.matmul(acc_a[0][:], zeros[:, :P], zeros[:], start=True, stop=True)
            pe.wait_ge(ident_ready, 1)
            turn_first()
            aggregate(0, 0)
            turn_second(0)
            turn_second(1)
            pe.wait_ge(w_lo_ready, 1)
            dense1(0, 0)
            pe.wait_ge(w_lo_ready, 3)
            turn_second(2)
            turn_second(3)
            support2(0, 0)
            with rounds(ENGINE.PE) as r:
                for u in range(SLOTS):
                    step(r, u)
            for b in range(LOOPED, B - 2):
                step(0, b)
            aggregate(0, B - 1)
            hidden2(0, B - 2)
            dense1(0, B - 1)
            support3(0, B - 2, SPREAD)
            support2(0, B - 1)
            output(0, B - 2, HALF_PARTS[:1])
            hidden2(0, B - 1)
            output(0, B - 2, HALF_PARTS[1:])
            support3(0, B - 1, SINGLE)
            pe.wait_ge(y_added, 2 * (B - 1))
            output_last()

        @block.scalar
        def _(act):
            def hi_of_turn(r, u, k):
                if isinstance(r, int) and u < 2:
                    source = (first_turned if u == 0 else turned * 2)[k]
                    act.wait_ge(turn_done, MT * u + k + 1)
                else:
                    source = turned[k % 2]
                    act.wait_ge(squares_turned, MT * graph(r, u - 2) + k + 1)
                nc.scalar.activation(adjT_hi[u % SLOTS][:, k], source[:], ACT.Copy).then_inc(adjT_hi_ready, 1)

            def hi_of(hi, acc, done, ready, c):
                for half in range(2):
                    act.wait_ge(done, 2 * c + half + 1)
                    nc.scalar.activation(hi[half], acc[half][:], ACT.Copy).then_inc(ready, 1)

            def relu_hi_of(hi, acc, bias, done, relu_done, ready, c):
                for half in range(2):
                    act.wait_ge(done, 2 * c + half + 1)
                    nc.scalar.activation(acc[half][:], acc[half][:], ACT.Relu, bias=bias[:, half:half + 1]
                                         ).then_inc(relu_done, 1)
                    act.wait_ge(relu_done, 2 * c + half + 1)
                    nc.scalar.activation(hi[half], acc[half][:], ACT.Copy).then_inc(ready, 1)

            rows = lambda t: [t[:, k] for k in range(FT)]
            nodes = lambda t: [t[:, h * PER_BANK:(h + 1) * PER_BANK].rearrange("p t f -> p (t f)")
                               for h in range(HALVES)]

            def ax(c):
                hi_of(rows(axT_hi), acc_a, ax_done, ax_hi_ready, c)

            def h1(c):
                relu_hi_of(rows(h1T_hi), acc_c, b1_col, h1_done, h1_relu_done, h1_hi_ready, c)

            def s2(c):
                hi_of(nodes(s2_hi), acc_b, s2_done, s2_hi_ready, c)

            def h2(c):
                relu_hi_of(rows(h2T_hi), acc_b, b2_col, h2_done, h2_relu_done, h2_hi_ready, c)

            def s3(c):
                hi_of(nodes(s3_hi), acc_a, s3_done, s3_hi_ready, c)

            def step(r, u, ahead, turning):
                b = graph(r, u)
                if ahead:
                    ax(b + 1)
                if turning:
                    hi_of_turn(r, u + 2, 0)
                    hi_of_turn(r, u + 2, 1)
                h2(b)
                if ahead:
                    h1(b + 1)
                s3(b)
                if ahead:
                    s2(b + 1)
                if turning:
                    hi_of_turn(r, u + 2, 2)
                    hi_of_turn(r, u + 2, 3)

            for k in range(MT):
                hi_of_turn(0, 0, k)
            for n in range(3):
                act.wait_ge(w_loaded[n], DMA)
                nc.scalar.activation(w_hi[:, n], w_raw[:, n], ACT.Copy).then_inc(w_hi_ready, 1)
            act.wait_ge(bias_loaded, 2 * DMA)
            ax(0)
            hi_of_turn(0, 1, 0)
            hi_of_turn(0, 1, 1)
            h1(0)
            hi_of_turn(0, 1, 2)
            hi_of_turn(0, 1, 3)
            s2(0)
            with rounds(ENGINE.Activation) as r:
                for u in range(SLOTS):
                    step(r, u, True, True)
            for b in range(LOOPED, B):
                step(0, b, b + 1 < B, b + 2 < B)
            i, tiles, _ = LAST_PARTS[-1]
            mine = slice(tiles.start, tiles.stop)
            act.wait_ge(y_normed, 2 * (B - 1) + i + 1)
            act.dma_start(out_dram[B - 1, :, mine], y[(B - 1) % SLOTS][:, mine]
                          ).then_inc(stored[(B - 1) % SLOTS], DMA)

        @block.vector
        def _(dve):
            def turn(r, u, k):
                s = u % SLOTS
                if k == 0:
                    dve.wait_ge(adj_loaded[s], QUADS * dma_count(r, u - 2))
                nc.vector.transpose(turned[k % 2][:], adj_raw[s][:, k]).then_inc(squares_turned, 1)

            def lo_of_turn(r, u, k):
                s, c = u % SLOTS, graph(r, u)
                source = first_turned[k] if isinstance(c, int) and c == 0 else turned[k % 2]
                dve.wait_ge(adjT_hi_ready, MT * c + k + 1)
                nc.vector.tensor_tensor(adjT_lo[s][:, k], source[:], adjT_hi[s][:, k].bitcast(F32),
                                        ALU.subtract).then_inc(adjT_lo_ready, 1)

            def turn_pair(r, u, k):
                for each in (turn, lo_of_turn):
                    each(r, u, k)
                    each(r, u, k + 1)

            def lo_of(lo, acc, hi, hi_ready, lo_ready, c):
                for half in range(2):
                    dve.wait_ge(hi_ready, 2 * c + half + 1)
                    nc.vector.tensor_tensor(lo[half], acc[half][:], hi[half].bitcast(F32), ALU.subtract
                                            ).then_inc(lo_ready, 1)

            rows = lambda t: [t[:, k] for k in range(FT)]
            nodes = lambda t: [t[:, h * PER_BANK:(h + 1) * PER_BANK].rearrange("p t f -> p (t f)")
                               for h in range(HALVES)]

            def ax(c):
                lo_of(rows(axT_lo), acc_a, rows(axT_hi), ax_hi_ready, ax_lo_ready, c)

            def h1(c):
                lo_of(rows(h1T_lo), acc_c, rows(h1T_hi), h1_hi_ready, h1_lo_ready, c)

            def s2(c):
                lo_of(nodes(s2_lo), acc_b, nodes(s2_hi), s2_hi_ready, s2_lo_ready, c)

            def h2(c):
                lo_of(rows(h2T_lo), acc_b, rows(h2T_hi), h2_hi_ready, h2_lo_ready, c)

            def s3(c):
                lo_of(nodes(s3_lo), acc_a, nodes(s3_hi), s3_hi_ready, s3_lo_ready, c)

            def hi_of_x(r, u):
                s, c = u % SLOTS, graph(r, u)
                dve.wait_ge(x_loaded[s], dma_count(r, u))
                if u > 0:
                    dve.wait_ge(ax_done, 2 * c)
                nc.vector.tensor_copy(x_hi[:], x_rows[s][:]).then_inc(x_hi_ready, 1)

            def add(r, u, parts):
                s, b = u % SLOTS, graph(r, u)
                for i, tiles, acc in parts:
                    mine = slice(tiles.start, tiles.stop)
                    dve.wait_ge(y_done, 2 * b + i + 1)
                    nc.vector.tensor_tensor(y[s][:, mine].rearrange("p t f -> p (t f)"), acc[:, :len(tiles) * F],
                                            x_rows[s][:, mine].rearrange("p t f -> p (t f)"), ALU.add
                                            ).then_inc(y_added, 1)
                    dve.wait_ge(y_added, 2 * b + i + 1)
                    for n in tiles:
                        nc.vector.bn_stats(stats[:, n], y[s][:, n]).then_inc(stats_done, 1)
                    dve.wait_ge(stats_done, MT * b + tiles.stop)
                    even, odd = stats[:, mine, 1], stats[:, mine, 4]
                    nc.vector.tensor_tensor(mean_gap[:, mine], even, odd, ALU.subtract).then_inc(pair_done, 1)
                    nc.vector.tensor_tensor(mean_sum[:, mine], even, odd, ALU.add).then_inc(pair_done, 1)
                    nc.vector.scalar_tensor_tensor(squares[:, mine], stats[:, mine, 2], F * EPS,
                                                   stats[:, mine, 5], ALU.add, ALU.add).then_inc(pair_done, 1)
                    dve.wait_ge(pair_done, 6 * b + 3 * i + 3)
                    nc.vector.scalar_tensor_tensor(gap_square[:, mine], mean_gap[:, mine], 0.25,
                                                   mean_gap[:, mine], ALU.mult, ALU.mult).then_inc(gap_done, 1)
                    nc.vector.tensor_scalar(mean[:, mine], mean_sum[:, mine], 0.5, None, ALU.mult
                                            ).then_inc(mean_ready, 1)
                    dve.wait_ge(gap_done, 2 * b + i + 1)
                    nc.vector.scalar_tensor_tensor(var_eps[:, mine], squares[:, mine], 1.0 / F,
                                                   gap_square[:, mine], ALU.mult, ALU.add
                                                   ).then_inc(var_ready, 1)

            def add_last(parts):
                s, b = (B - 1) % SLOTS, B - 1
                for i, tiles, acc in parts:
                    n = tiles[0]
                    dve.wait_ge(y_done, 2 * b + i + 1)
                    nc.vector.tensor_tensor(y[s][:, n], acc[:, :F], x_rows[s][:, n], ALU.add).then_inc(y_added, 1)
                    dve.wait_ge(y_added, 2 * b + i + 1)
                    nc.vector.bn_stats(stats[:, n], y[s][:, n]).then_inc(stats_done, 1)
                    dve.wait_ge(stats_done, MT * b + n + 1)
                    nc.vector.bn_aggr(mean_var[:, n], stats[:, n]).then_inc(mean_ready, 1)
                    dve.wait_ge(mean_ready, 2 * b + i + 1)
                    nc.vector.tensor_scalar(var_eps[:, n:n + 1], mean_var[:, n, 1:2], EPS, None, ALU.add
                                            ).then_inc(var_ready, 1)

            def scale(r, u, parts, mean):
                s, b = u % SLOTS, graph(r, u)
                for i, tiles, _ in parts:
                    dve.wait_ge(mean_ready, 2 * b + i + 1)
                    dve.wait_ge(rstd_ready, 2 * b + i + 1)
                    for n in tiles:
                        last = nc.vector.tensor_scalar(y[s][:, n], y[s][:, n], mean[:, n:n + 1],
                                                       rstd[:, n:n + 1], ALU.subtract, ALU.mult)
                    last.then_inc(y_normed, 1)

            def step(r, u, turning):
                b = graph(r, u)
                ax(b + 1)
                if turning:
                    turn_pair(r, u + 2, 0)
                h2(b)
                h1(b + 1)
                if turning:
                    hi_of_x(r, u + 2)
                s3(b)
                s2(b + 1)
                if turning:
                    turn_pair(r, u + 2, 2)
                dve.wait_ge(x_biased, b + 1)
                add(r, u, HALF_PARTS)
                scale(r, u, HALF_PARTS, mean)

            nc.vector.memset(zeros[:], 0.0).then_inc(zeros_ready, 1)
            for t, loaded in enumerate(x_tile_loaded + x_loaded[:1]):
                dve.wait_ge(loaded, DMA)
                nc.vector.tensor_copy(x_hi[:, t], x_rows[0][:, t]
                                      ).then_inc(x_tile_hi_ready if t < MT - 1 else x_hi_ready, 1)
                if t == MT - 2:
                    lo_of_turn(0, 0, 0)
            for k in range(1, MT):
                lo_of_turn(0, 0, k)
            for n in range(3):
                dve.wait_ge(w_hi_ready, n + 1)
                nc.vector.tensor_tensor(w_lo[:, n], w_raw[:, n], w_hi[:, n].bitcast(F32), ALU.subtract
                                        ).then_inc(w_lo_ready, 1)
            ax(0)
            lo_of_turn(0, 1, 0)
            lo_of_turn(0, 1, 1)
            hi_of_x(0, 1)
            h1(0)
            lo_of_turn(0, 1, 2)
            lo_of_turn(0, 1, 3)
            s2(0)
            with rounds(ENGINE.DVE) as r:
                for u in range(SLOTS):
                    step(r, u, True)
            for b in range(LOOPED, B - 2):
                step(0, b, True)
            ax(B - 1)
            h2(B - 2)
            h1(B - 1)
            s3(B - 2)
            s2(B - 1)
            dve.wait_ge(x_biased, B - 1)
            for b in (B - 2, B - 1):
                dve.wait_ge(stored[b % SLOTS], 2 * dma_count(0, b - SLOTS))
            add(0, B - 2, HALF_PARTS[:1])
            h2(B - 1)
            add(0, B - 2, HALF_PARTS[1:])
            s3(B - 1)
            scale(0, B - 2, HALF_PARTS, mean)
            dve.wait_ge(x_biased, B)
            last_mean = mean_var[:, :, 0]
            add_last(LAST_PARTS)
            scale(0, B - 1, LAST_PARTS, last_mean)


def kernel(x, adj, L0_gnn_W1, L0_gnn_b1, L0_gnn_W2, L0_gnn_b2, L0_gnn_W3, L0_gnn_b3):
    import numpy as np
    import concourse.bacc as bacc
    from concourse.bass_utils import run_bass_kernel_spmd

    nc = bacc.Bacc("TRN2", target_bir_lowering=False, num_devices=1)
    inputs = {"x": x, "adj": adj, "W1": L0_gnn_W1, "b1": L0_gnn_b1, "W2": L0_gnn_W2, "b2": L0_gnn_b2,
              "W3": L0_gnn_W3, "b3": L0_gnn_b3}
    arrays, args = {}, []
    for name, value in inputs.items():
        a = np.ascontiguousarray(value)
        arrays[f"in_{name}"] = a
        args.append(nc.dram_tensor(f"in_{name}", a.shape, mybir.dt.from_np(a.dtype), kind="ExternalInput").ap())
    args.append(nc.dram_tensor("out_y", x.shape, F32, kind="ExternalOutput").ap())
    gcn_resnorm(nc, *args)
    result = run_bass_kernel_spmd(nc, [arrays], core_ids=[0])
    return result.results[0]["out_y"]
```
